# Optimizing a Trainium2 kernel written in Bass

```python
import numpy as np
import jax
import jax.numpy as jnp

def _softmax(x, axis=-1):
    return jax.nn.softmax(x, axis=axis)

def _gelu(x):
    return jax.nn.gelu(x, approximate=True)

def _silu(x):
    return jax.nn.silu(x)

def _sigmoid(x):
    return jax.nn.sigmoid(x)

def _layernorm(x, axis=-1, eps=1e-05):
    m = jnp.mean(x, axis=axis, keepdims=True)
    v = jnp.var(x, axis=axis, keepdims=True)
    return (x - m) / jnp.sqrt(v + eps)

def _scatter_add(tgt, idx, src, axis=0):
    return tgt.at[idx].add(src)

def _segment_sum(src, seg, n):
    return jax.ops.segment_sum(src, seg, n)
kernel_name = 'mk_dlrm_tower_d1_rec_r8_bba43b'

def setup_inputs(seed: int=0):
    np.random.seed(seed)
    _w = jnp.asarray

    def _rec_inputs():
        import jax
        import jax.numpy as jnp
        _tk = jax.random.key(seed)
        ids = jnp.stack([jax.random.randint(jax.random.fold_in(_tk, 200 + f), (2048,), 0, v, jnp.int32) for f, v in enumerate([1250, 12500, 125000, 1250, 1000, 1000, 1250, 1250, 1250, 1250, 1000, 1000, 1250, 12500, 1250, 1000, 1000, 1000, 1000, 1250, 1000, 1000, 1250, 1250, 12500, 12500])], axis=1)
        tbl_0 = 0.05 * jax.random.normal(jax.random.fold_in(_tk, 500 + 0), (1250, 128), jnp.float32)
        tbl_1 = 0.05 * jax.random.normal(jax.random.fold_in(_tk, 500 + 1), (12500, 128), jnp.float32)
        tbl_2 = 0.05 * jax.random.normal(jax.random.fold_in(_tk, 500 + 2), (125000, 128), jnp.float32)
        tbl_3 = 0.05 * jax.random.normal(jax.random.fold_in(_tk, 500 + 3), (1250, 128), jnp.float32)
        tbl_4 = 0.05 * jax.random.normal(jax.random.fold_in(_tk, 500 + 4), (1000, 128), jnp.float32)
        tbl_5 = 0.05 * jax.random.normal(jax.random.fold_in(_tk, 500 + 5), (1000, 128), jnp.float32)
        tbl_6 = 0.05 * jax.random.normal(jax.random.fold_in(_tk, 500 + 6), (1250, 128), jnp.float32)
        tbl_7 = 0.05 * jax.random.normal(jax.random.fold_in(_tk, 500 + 7), (1250, 128), jnp.float32)
        tbl_8 = 0.05 * jax.random.normal(jax.random.fold_in(_tk, 500 + 8), (1250, 128), jnp.float32)
        tbl_9 = 0.05 * jax.random.normal(jax.random.fold_in(_tk, 500 + 9), (1250, 128), jnp.float32)
        tbl_10 = 0.05 * jax.random.normal(jax.random.fold_in(_tk, 500 + 10), (1000, 128), jnp.float32)
        tbl_11 = 0.05 * jax.random.normal(jax.random.fold_in(_tk, 500 + 11), (1000, 128), jnp.float32)
        tbl_12 = 0.05 * jax.random.normal(jax.random.fold_in(_tk, 500 + 12), (1250, 128), jnp.float32)
        tbl_13 = 0.05 * jax.random.normal(jax.random.fold_in(_tk, 500 + 13), (12500, 128), jnp.float32)
        tbl_14 = 0.05 * jax.random.normal(jax.random.fold_in(_tk, 500 + 14), (1250, 128), jnp.float32)
        tbl_15 = 0.05 * jax.random.normal(jax.random.fold_in(_tk, 500 + 15), (1000, 128), jnp.float32)
        tbl_16 = 0.05 * jax.random.normal(jax.random.fold_in(_tk, 500 + 16), (1000, 128), jnp.float32)
        tbl_17 = 0.05 * jax.random.normal(jax.random.fold_in(_tk, 500 + 17), (1000, 128), jnp.float32)
        tbl_18 = 0.05 * jax.random.normal(jax.random.fold_in(_tk, 500 + 18), (1000, 128), jnp.float32)
        tbl_19 = 0.05 * jax.random.normal(jax.random.fold_in(_tk, 500 + 19), (1250, 128), jnp.float32)
        tbl_20 = 0.05 * jax.random.normal(jax.random.fold_in(_tk, 500 + 20), (1000, 128), jnp.float32)
        tbl_21 = 0.05 * jax.random.normal(jax.random.fold_in(_tk, 500 + 21), (1000, 128), jnp.float32)
        tbl_22 = 0.05 * jax.random.normal(jax.random.fold_in(_tk, 500 + 22), (1250, 128), jnp.float32)
        tbl_23 = 0.05 * jax.random.normal(jax.random.fold_in(_tk, 500 + 23), (1250, 128), jnp.float32)
        tbl_24 = 0.05 * jax.random.normal(jax.random.fold_in(_tk, 500 + 24), (12500, 128), jnp.float32)
        tbl_25 = 0.05 * jax.random.normal(jax.random.fold_in(_tk, 500 + 25), (12500, 128), jnp.float32)
        _rk = jax.random.fold_in(_tk, 7)
        r_dense_features = -0.000520686 + 1.00062 * jax.random.normal(jax.random.fold_in(_rk, 101), (2048, 128), jnp.float32)
        W_top1 = 0.0405887 * jax.random.normal(jax.random.fold_in(_tk, 801), (607, 512), jnp.float32)
        W_top2 = 0.0441942 * jax.random.normal(jax.random.fold_in(_tk, 802), (512, 256), jnp.float32)
        W_top3 = 0.0625 * jax.random.normal(jax.random.fold_in(_tk, 803), (256, 1), jnp.float32)
        b_top1 = jnp.zeros((512,), jnp.float32)
        b_top2 = jnp.zeros((256,), jnp.float32)
        return (r_dense_features, ids, tbl_0, tbl_1, tbl_2, tbl_3, tbl_4, tbl_5, tbl_6, tbl_7, tbl_8, tbl_9, tbl_10, tbl_11, tbl_12, tbl_13, tbl_14, tbl_15, tbl_16, tbl_17, tbl_18, tbl_19, tbl_20, tbl_21, tbl_22, tbl_23, tbl_24, tbl_25, W_top1, b_top1, W_top2, b_top2, W_top3)
    r_dense_features, ids, tbl_0, tbl_1, tbl_2, tbl_3, tbl_4, tbl_5, tbl_6, tbl_7, tbl_8, tbl_9, tbl_10, tbl_11, tbl_12, tbl_13, tbl_14, tbl_15, tbl_16, tbl_17, tbl_18, tbl_19, tbl_20, tbl_21, tbl_22, tbl_23, tbl_24, tbl_25, W_top1, b_top1, W_top2, b_top2, W_top3 = _rec_inputs()

    def _L0_rec_setup():
        import jax, jax.numpy as jnp
        import numpy as np
        NUM_SPARSE = 26
        EMBED_DIM = 128
        BATCH = 2048
        key = jax.random.key(seed)
        k1, k2 = jax.random.split(key)
        dense_features = jax.random.normal(k1, (BATCH, EMBED_DIM), dtype=jnp.float32)
        sparse_features = jax.random.normal(k2, (BATCH, NUM_SPARSE, EMBED_DIM), dtype=jnp.float32)
        return {'dense_features': dense_features, 'sparse_features': sparse_features}
    _L0_rec_all = _L0_rec_setup()
    _L0_rec_in = {k: v for k, v in _L0_rec_all.items() if k in ()}
    del _L0_rec_all
    return {'r_dense_features': r_dense_features, 'ids': ids, 'tbl_0': tbl_0, 'tbl_1': tbl_1, 'tbl_2': tbl_2, 'tbl_3': tbl_3, 'tbl_4': tbl_4, 'tbl_5': tbl_5, 'tbl_6': tbl_6, 'tbl_7': tbl_7, 'tbl_8': tbl_8, 'tbl_9': tbl_9, 'tbl_10': tbl_10, 'tbl_11': tbl_11, 'tbl_12': tbl_12, 'tbl_13': tbl_13, 'tbl_14': tbl_14, 'tbl_15': tbl_15, 'tbl_16': tbl_16, 'tbl_17': tbl_17, 'tbl_18': tbl_18, 'tbl_19': tbl_19, 'tbl_20': tbl_20, 'tbl_21': tbl_21, 'tbl_22': tbl_22, 'tbl_23': tbl_23, 'tbl_24': tbl_24, 'tbl_25': tbl_25, 'W_top1': W_top1, 'b_top1': b_top1, 'W_top2': W_top2, 'b_top2': b_top2, 'W_top3': W_top3}

def reference(r_dense_features, ids, tbl_0, tbl_1, tbl_2, tbl_3, tbl_4, tbl_5, tbl_6, tbl_7, tbl_8, tbl_9, tbl_10, tbl_11, tbl_12, tbl_13, tbl_14, tbl_15, tbl_16, tbl_17, tbl_18, tbl_19, tbl_20, tbl_21, tbl_22, tbl_23, tbl_24, tbl_25, W_top1, b_top1, W_top2, b_top2, W_top3):
    import jax
    import jax.numpy as jnp

    def _L0_rec_ref(dense_features, sparse_features):
        import jax, jax.numpy as jnp
        import numpy as np
        NUM_SPARSE = 26
        EMBED_DIM = 128
        BATCH = 2048
        F = NUM_SPARSE + 1
        combined = jnp.concatenate([dense_features[:, None, :], sparse_features], axis=1)
        interactions = jnp.einsum('bfd,bgd->bfg', combined, combined)
        iu, ju = jnp.triu_indices(F, k=1)
        interactions_flat = interactions[:, iu, ju]
        return jnp.concatenate([dense_features, interactions_flat], axis=1)
    e = jnp.stack([tbl_0[ids[:, 0]], tbl_1[ids[:, 1]], tbl_2[ids[:, 2]], tbl_3[ids[:, 3]], tbl_4[ids[:, 4]], tbl_5[ids[:, 5]], tbl_6[ids[:, 6]], tbl_7[ids[:, 7]], tbl_8[ids[:, 8]], tbl_9[ids[:, 9]], tbl_10[ids[:, 10]], tbl_11[ids[:, 11]], tbl_12[ids[:, 12]], tbl_13[ids[:, 13]], tbl_14[ids[:, 14]], tbl_15[ids[:, 15]], tbl_16[ids[:, 16]], tbl_17[ids[:, 17]], tbl_18[ids[:, 18]], tbl_19[ids[:, 19]], tbl_20[ids[:, 20]], tbl_21[ids[:, 21]], tbl_22[ids[:, 22]], tbl_23[ids[:, 23]], tbl_24[ids[:, 24]], tbl_25[ids[:, 25]]], axis=1)
    z = _L0_rec_ref(r_dense_features, e)
    z = z.reshape(z.shape[0], -1)
    h = jnp.concatenate([z, r_dense_features], axis=1)
    h = jnp.maximum(h @ W_top1 + b_top1, 0.0)
    h = jnp.maximum(h @ W_top2 + b_top2, 0.0)
    y = h @ W_top3
    return y

_drawn_inputs = setup_inputs


def setup_inputs(seed=0):
    import zlib

    import numpy as np

    out = dict(_drawn_inputs(seed))
    spreads = {'b_top1': (0.0, 0.1), 'b_top2': (0.0, 0.1)}
    factors = {}
    for name, (base, spread) in spreads.items():
        noise = np.random.default_rng([zlib.crc32(name.encode()), seed]).standard_normal(out[name].shape)
        drawn = base * np.exp(spread * noise) if base else spread * noise
        out[name] = jnp.asarray(drawn.astype(out[name].dtype))
    for name, factor in factors.items():
        out[name] = (out[name] * factor).astype(out[name].dtype)
    return out
```

```python
from contextlib import ExitStack

import concourse.bass as bass
from concourse import mybir

P = 128
F32 = mybir.dt.float32
U32 = mybir.dt.uint32
ALU = mybir.AluOpType
ACT = mybir.ActivationFunctionType

QUAD = 32
NJ = P // QUAD
PAIR = 2
SLOTS = 2 * PAIR
GROUP = 4
DMA = 16


def build_dlrm(nc, dense, ids, tables, w1, b1, w2, b2, w3, out):
    B, D = dense.shape
    NT = len(tables)
    F = NT + 1
    N1, N2 = w1.shape[1], w2.shape[1]
    C1, C2 = N1 // P, N2 // P
    NPAIR = F * (F - 1) // 2
    TURNS = B // (P * SLOTS)
    COLS = PAIR * P
    QT = QUAD * PAIR
    HALF = QUAD // 2
    GROUPS = -(-F // GROUP)
    assert D == P and B == TURNS * P * SLOTS and (GROUPS * SLOTS) % 2 == 0

    chunks, rows, at = [[0, 0]], [], 0
    for f in range(F - 1):
        n = F - 1 - f
        if chunks[-1][1] + n > P:
            chunks.append([at, 0])
        rows.append((f, n, len(chunks) - 1, chunks[-1][1]))
        chunks[-1][1] += n
        at += n
    ZC = len(chunks)
    assert at == NPAIR

    with ExitStack() as ctx:
        def sb(name, shape, dt=F32):
            return ctx.enter_context(nc.sbuf_tensor(name, shape, dt))

        def ps(name, shape):
            return ctx.enter_context(nc.psum_tensor(name, shape, F32))

        def sem(name):
            return ctx.enter_context(nc.semaphore(name))

        idx = sb("idx", [P, SLOTS, NT], U32)
        rows_sb = sb("rows_sb", [P, SLOTS, F, D])
        xt = sb("xt", [P, SLOTS, P, F])
        gram_sb = sb("gram_sb", [P, 2, F, QT])
        z_sb = sb("z_sb", [P, 2, ZC, COLS])
        w1z = sb("w1z", [P, ZC, N1])
        w1d = sb("w1d", [P, 2, N1])
        w1s = sb("w1s", [P, N1])
        w2_sb = sb("w2_sb", [P, C1, N2])
        w3_sb = sb("w3_sb", [P, C2])
        b1_sb = sb("b1_sb", [P, C1])
        b2_sb = sb("b2_sb", [P, C2])
        h1 = sb("h1", [P, C1, COLS])
        h2 = sb("h2", [P, C2, COLS])
        y_sb = sb("y_sb", [1, 2, COLS])
        ones = sb("ones", [P, P])
        ident = sb("ident", [P, P])
        turn_ps = ps("turn_ps", [P, 2, 512])
        gram_ps = ps("gram_ps", [P, 2, 512])
        mlp_ps = ps("mlp_ps", [P, 2, 512])
        y_ps = ps("y_ps", [P, 512])

        weights_in = sem("weights_in")
        w1s_ready = sem("w1s_ready")
        ones_ready = sem("ones_ready")
        ident_ready = sem("ident_ready")
        gram_cleared = sem("gram_cleared")
        idx_in = [sem(f"idx_in{s}") for s in range(SLOTS)]
        dense_in = [sem(f"dense_in{s}") for s in range(SLOTS)]
        gathered = [sem(f"gathered{s}") for s in range(SLOTS)]
        turned = sem("turned")
        xt_by = [sem("xt_by_act"), sem("xt_by_dve")]
        gram_ready = sem("gram_ready")
        gram_copied = sem("gram_copied")
        z_out = [sem("z_out0"), sem("z_out1")]
        z_in = [sem("z_in0"), sem("z_in1")]
        mlp_ready = sem("mlp_ready")
        mlp_copied = sem("mlp_copied")
        y_ready = sem("y_ready")
        y_copied = sem("y_copied")
        y_out = [sem("y_out0"), sem("y_out1")]

        z_dram = nc.dram_tensor("z_dram", (2, F, F, NJ, QT), F32, kind="Internal").ap()

        out_v = out.rearrange("(i a j q) o -> i j a (q o)", a=PAIR, j=NJ, q=QUAD)
        xt_pair = xt[:, :, :, :].rearrange("d (h a) (j q) f -> d h f j a q", a=PAIR, j=NJ)
        w1s_c = w1s[:, :].rearrange("d (p c) -> d c p", c=C1)
        w1z_c = w1z[:, :, :].rearrange("d k (p c) -> d k c p", c=C1)
        w2_c = w2_sb[:, :, :].rearrange("d k (p c) -> d k c p", c=C2)

        NW = ZC + 6
        block = ctx.enter_context(nc.Block())

        def group_index(s, g):
            return GROUPS * s + g

        def before(bank, k, S):
            return S * (GROUPS * SLOTS // 2) + (k + 1 - bank) // 2

        @block.sync
        def _(sp):
            def load_tile(S, s, first):
                t = S * SLOTS + s
                if not first:
                    sp.wait_ge(gathered[s], S * (DMA * NT))
                    sp.nop(nofuse=True)
                sp.dma_start(idx[:, s, :], ids[bass.ds(t * P, P), :].bitcast(U32)).then_inc(idx_in[s], DMA)
                if not first:
                    sp.wait_ge(turned, (S - 1) * (GROUPS * SLOTS) + GROUPS * (s + 1))
                    sp.nop(nofuse=True)
                sp.dma_start(rows_sb[:, s, 0, :], dense[bass.ds(t * P, P), :]).then_inc(dense_in[s], DMA)

            def move_z(S, h, first):
                sp.wait_ge(gram_copied, S * (2 * SLOTS) + 2 * PAIR * (h + 1))
                sp.nop(nofuse=True)
                if not first:
                    sp.wait_ge(z_in[h], S * (DMA * len(rows)))
                    sp.nop(nofuse=True)
                for j in range(NJ):
                    sp.dma_start(z_dram[h, :, :, j, :], gram_sb[j * QUAD:j * QUAD + F, h, :, :]).then_inc(z_out[h], DMA)
                sp.wait_ge(z_out[h], (S + 1) * (DMA * NJ))
                sp.nop(nofuse=True)
                if not first:
                    sp.wait_ge(mlp_ready, (2 * S + h - 2) * (C1 + C2) + C1)
                    sp.nop(nofuse=True)
                for f, n, c, p0 in rows:
                    sp.dma_start(z_sb[p0:p0 + n, h, c, :],
                                 z_dram[h, f, f + 1:F, :, :].rearrange("g j q -> g (j q)")).then_inc(z_in[h], DMA)

            def store_y(S, h):
                sp.wait_ge(y_copied, 2 * S + h + 1)
                sp.nop(nofuse=True)
                sp.dma_start(out_v[bass.ds(2 * S + h, 1)],
                             y_sb[0:1, h, :].rearrange("o (j a q) -> o j a q", j=NJ, a=PAIR)).then_inc(y_out[h], DMA)

            for s in range(SLOTS):
                load_tile(0, s, True)
            for a, b in ((w1d[:, 0, :], w1[0:D, :]), (w1d[:, 1, :], w1[D + NPAIR:2 * D + NPAIR, :]),
                         (w2_sb[:, :, :], w2.rearrange("(p c) n -> p c n", c=C1)),
                         (w3_sb[:, :], w3.rearrange("(p c) o -> p (c o)", c=C2)),
                         (b1_sb[:, :], b1.rearrange("(p c) -> p c", c=C1)),
                         (b2_sb[:, :], b2.rearrange("(p c) -> p c", c=C2))):
                sp.dma_start(a, b).then_inc(weights_in, DMA)
            for c, (r0, n) in enumerate(chunks):
                sp.dma_start(w1z[0:n, c, :], w1[D + r0:D + r0 + n, :]).then_inc(weights_in, DMA)

            def pair(S, h, first, last):
                if not last:
                    for a in range(PAIR):
                        load_tile(S + 1, h * PAIR + a, False)
                move_z(S, h, first)

            pair(0, 0, True, False)
            pair(0, 1, True, False)
            store_y(0, 0)
            with sp.Fori(1, TURNS - 1) as S:
                pair(S, 0, False, False)
                store_y(S - 1, 1)
                pair(S, 1, False, False)
                store_y(S, 0)
            pair(TURNS - 1, 0, False, True)
            store_y(TURNS - 2, 1)
            pair(TURNS - 1, 1, False, True)
            store_y(TURNS - 1, 0)
            store_y(TURNS - 1, 1)
            for h in range(2):
                sp.wait_ge(y_out[h], TURNS * DMA)
                sp.nop(nofuse=True)

        @block.gpsimd
        def _(gp):
            gp.memset(ones[:, :], 1.0).then_inc(ones_ready, 1)
            gp.wait_ge(ones_ready, 1)
            gp.affine_select(ident[:, :], ones[:, :], pattern=[[-1, P]], compare_op=ALU.is_equal, fill=0.0,
                             base=0, channel_multiplier=1).then_inc(ident_ready, 1)

            def gather(S, s, first):
                gp.wait_ge(idx_in[s], (S + 1) * DMA)
                if not first:
                    gp.wait_ge(turned, (S - 1) * (GROUPS * SLOTS) + GROUPS * (s + 1))
                    gp.nop(nofuse=True)
                for f in range(NT):
                    gp.indirect_dma_start(
                        out=rows_sb[:, s, f + 1, :], out_offset=None, in_=tables[f],
                        in_offset=bass.IndirectOffsetOnAxis(ap=idx[:, s, f:f + 1], axis=0)
                    ).then_inc(gathered[s], DMA)

            for s in range(SLOTS):
                gather(0, s, True)
            with gp.Fori(1, TURNS) as S:
                for s in range(SLOTS):
                    gather(S, s, False)

        def copy_turned(eng, copy, bank, S, s):
            for g in range(GROUPS):
                k = group_index(s, g)
                if k % 2 == bank:
                    n = min(GROUP, F - g * GROUP)
                    eng.wait_ge(turned, S * (GROUPS * SLOTS) + k + 1)
                    copy(xt[:, s, :, g * GROUP:g * GROUP + n].rearrange("d p f -> d f p"),
                         turn_ps[:, bank, 0:n * P].rearrange("d (f p) -> d f p", p=P)).then_inc(xt_by[bank], 1)

        @block.scalar
        def _(act):
            def mlp(S, h, first):
                U = C1 + C2
                base = S * (2 * U) + h * U
                for u in range(U):
                    act.wait_ge(mlp_ready, base + u + 1)
                    dst, bias = (h1[:, u, :], b1_sb[:, u:u + 1]) if u < C1 else (h2[:, u - C1, :], b2_sb[:, u - C1:u - C1 + 1])
                    act.activation(dst, mlp_ps[:, u % 2, 0:COLS], ACT.Relu, bias=bias).then_inc(mlp_copied, 1)
                act.wait_ge(y_ready, 2 * S + h + 1)
                if not first:
                    act.wait_ge(y_out[h], S * DMA)
                act.copy(y_sb[0:1, h, :], y_ps[0:1, 0:COLS]).then_inc(y_copied, 1)

            def front(S, h):
                for a in range(PAIR):
                    copy_turned(act, act.copy, 0, S, h * PAIR + a)

            act.wait_ge(weights_in, NW * DMA)
            front(0, 0)
            front(0, 1)
            mlp(0, 0, True)
            front(1, 0)
            mlp(0, 1, True)
            front(1, 1)
            mlp(1, 0, False)
            with act.Fori(2, TURNS) as S:
                front(S, 0)
                mlp(S - 1, 1, False)
                front(S, 1)
                mlp(S, 0, False)
            mlp(TURNS - 1, 1, False)

        @block.vector
        def _(dve):
            for b in range(2):
                dve.memset(gram_ps[:, b, 0:HALF * F], 0.0).then_inc(gram_cleared, 1)

            def tile(S, s, first):
                h, a = s // PAIR, s % PAIR
                copy_turned(dve, dve.tensor_copy, 1, S, s)
                if a == 0 and not first:
                    dve.wait_ge(z_out[h], S * (DMA * NJ))
                for b in range(2):
                    dve.wait_ge(gram_ready, S * (2 * SLOTS) + 2 * s + b + 1)
                    q0 = a * QUAD + b * HALF
                    dve.tensor_copy(gram_sb[:, h, :, q0:q0 + HALF],
                                    gram_ps[:, b, 0:HALF * F].rearrange("p (q g) -> p g q", g=F)
                                    ).then_inc(gram_copied, 1)

            tile(0, 0, True)
            dve.wait_ge(weights_in, NW * DMA)
            dve.tensor_tensor(w1s[:, :], w1d[:, 0, :], w1d[:, 1, :], ALU.add).then_inc(w1s_ready, 1)
            for s in range(1, SLOTS):
                tile(0, s, True)
            with dve.Fori(1, TURNS) as S:
                for s in range(SLOTS):
                    tile(S, s, False)

        @block.tensor
        def _(pe):
            def turn(S, s, first):
                pe.wait_ge(gathered[s], (S + 1) * (DMA * NT))
                pe.wait_ge(dense_in[s], (S + 1) * DMA)
                for g in range(GROUPS):
                    k = group_index(s, g)
                    bank = k % 2
                    if not (first and k < 2):
                        pe.wait_ge(xt_by[bank], before(bank, k, S))
                    n = min(GROUP, F - g * GROUP)
                    for i in range(n):
                        mm = pe.transpose(turn_ps[:, bank, i * P:(i + 1) * P],
                                          rows_sb[:, s, g * GROUP + i, :], ident[:, :])
                    mm.then_inc(turned, 1)

            def grams(S, s, first):
                for bank in range(2):
                    pe.wait_ge(xt_by[bank], before(bank, group_index(s, GROUPS), S))
                for b in range(2):
                    if not (first and s == 0):
                        pe.wait_ge(gram_copied, S * (2 * SLOTS) + 2 * s + b - 1)
                    for q in range(HALF):
                        for j in range(NJ):
                            p = j * QUAD + b * HALF + q
                            mm = pe.matmul(gram_ps[j * QUAD:j * QUAD + F, b, q * F:(q + 1) * F],
                                           xt[:, s, p, :], xt[:, s, p, :], start=True, stop=True,
                                           tile_position=(0, j * QUAD))
                    mm.then_inc(gram_ready, 1)

            def front(S, h, first):
                for a in range(PAIR):
                    turn(S, h * PAIR + a, first)
                    grams(S, h * PAIR + a, first)

            def mlp(S, h, first):
                U = C1 + C2
                base = S * (2 * U) + h * U
                pe.wait_ge(z_in[h], (S + 1) * (DMA * len(rows)))
                for u in range(U):
                    if not (first and u < 2):
                        pe.wait_ge(mlp_copied, base + u - 1)
                    o = mlp_ps[:, u % 2, 0:COLS]
                    if u < C1:
                        for c, (r0, n) in enumerate(chunks):
                            pe.matmul(o, w1z_c[0:n, c, u, :], z_sb[0:n, h, c, :], start=(c == 0), stop=False)
                        mm = pe.matmul(o, w1s_c[:, u, :], xt_pair[:, h, 0, :, :, :], start=False, stop=True)
                    else:
                        if u == C1:
                            pe.wait_ge(mlp_copied, base + C1)
                        for c in range(C1):
                            mm = pe.matmul(o, w2_c[:, c, u - C1, :], h1[:, c, :], start=(c == 0), stop=(c == C1 - 1))
                    mm.then_inc(mlp_ready, 1)
                pe.wait_ge(mlp_copied, base + U)
                if not first:
                    pe.wait_ge(y_copied, 2 * S + h)
                for c in range(C2):
                    mm = pe.matmul(y_ps[0:1, 0:COLS], w3_sb[:, c:c + 1], h2[:, c, :], start=(c == 0), stop=(c == C2 - 1))
                mm.then_inc(y_ready, 1)

            pe.wait_ge(ident_ready, 1)
            pe.wait_ge(gram_cleared, 2)
            front(0, 0, True)
            front(0, 1, True)
            pe.wait_ge(weights_in, NW * DMA)
            pe.wait_ge(w1s_ready, 1)
            mlp(0, 0, True)
            with pe.Fori(1, TURNS) as S:
                front(S, 0, False)
                mlp(S - 1, 1, False)
                front(S, 1, False)
                mlp(S, 0, False)
            mlp(TURNS - 1, 1, False)


def kernel(**inputs):
    import numpy as np
    import concourse.bacc as bacc
    from concourse.bass_utils import run_bass_kernel_spmd as run

    nc = bacc.Bacc("TRN2", target_bir_lowering=False, num_devices=1)
    arrays, aps = {}, {}
    for name, a in inputs.items():
        a = np.ascontiguousarray(a)
        arrays["in_" + name] = a
        aps[name] = nc.dram_tensor("in_" + name, a.shape, mybir.dt.from_np(a.dtype), kind="ExternalInput").ap()
    B, NT = inputs["ids"].shape
    out = nc.dram_tensor("out", (B, 1), F32, kind="ExternalOutput").ap()
    build_dlrm(nc, aps["r_dense_features"], aps["ids"], [aps[f"tbl_{i}"] for i in range(NT)],
               aps["W_top1"], aps["b_top1"], aps["W_top2"], aps["b_top2"], aps["W_top3"], out)
    r = run(nc, [arrays], core_ids=[0])
    return r.results[0]["out"]
```

```python
from contextlib import ExitStack

import concourse.bass as bass
from concourse import mybir

P = 128
F32 = mybir.dt.float32
F32R = mybir.dt.float32r
I32 = mybir.dt.int32
U32 = mybir.dt.uint32
ALU = mybir.AluOpType
ACT = mybir.ActivationFunctionType

SELECTED = 9
QUAD = 32
NJ = P // QUAD
PAIR = 2
GROUP = 4
EARLY = 2
PARTS = 3
DMA = 16


def feature_order(sizes):
    least = min(sizes)
    chosen = [t for t, v in enumerate(sizes) if v == least][:SELECTED]
    return [t for t in range(len(sizes)) if t not in chosen], chosen


def pair_order(F):
    blocks, pairs = [], []
    for k in range(1, (F + 1) // 2 + 1):
        f0 = F // 2 if k == (F + 1) // 2 else 0
        blocks.append(((F + 1) * f0 + k, F - 1 - f0))
        for f in range(f0, F - 1):
            a, b = divmod((F + 1) * f + k, F)
            pairs.append((min(a, b), max(a, b)))
    assert F % 2 == 1 and len(set(pairs)) == len(pairs) == F * (F - 1) // 2
    return blocks, pairs


def build_dlrm(nc, dense, ids_rows, ids_cols, gathered_tables, selected_tables, w1, b1, w2, b2, w3, out):
    B, D = dense.shape
    NG, NS = len(gathered_tables), len(selected_tables)
    R = 1 + NG
    F = R + NS
    N1, N2 = w1.shape[1], w2.shape[1]
    C1, C2 = N1 // P, N2 // P
    NPAIR = F * (F - 1) // 2
    COLS = PAIR * P
    TURNS = B // COLS
    QT = QUAD * PAIR
    HALF = QUAD // 2
    GROUPS = -(-R // GROUP)
    V = selected_tables[0].shape[0]
    VC = -(-V // P)
    VP = V // VC
    VH = VC // 2
    ZC = -(-NPAIR // P)
    ZP = NPAIR // ZC
    U = C1 + C2 + 1
    assert D == P and B == TURNS * COLS and V == VC * VP and VC == 2 * VH and 2 * NS % PARTS == 0 and NPAIR == ZC * ZP

    blocks, _ = pair_order(F)
    runs, at = [], 0
    for e0, n in blocks:
        while n:
            m = min(n, ZP - at % ZP)
            runs.append((e0, m, at // ZP, at % ZP))
            e0, n, at = e0 + m * (F + 1), n - m, at + m

    with ExitStack() as ctx:
        def sb(name, shape, dt=F32):
            return ctx.enter_context(nc.sbuf_tensor(name, shape, dt))

        def ps(name, shape):
            return ctx.enter_context(nc.psum_tensor(name, shape, F32))

        def sem(name):
            return ctx.enter_context(nc.semaphore(name))

        idx = sb("idx", [P, PAIR, NG], U32)
        rows_sb = sb("rows_sb", [P, PAIR, R, D])
        ids_sb = sb("ids_sb", [VP, NS, COLS], I32)
        row_ids = sb("row_ids", [VP, VC], I32)
        row_ids_f = sb("row_ids_f", [VP, VC])
        stage = sb("stage", [P, 2, VC * D])
        tab_hi = sb("tab_hi", [VP, NS, VC * D], F32R)
        tab_lo = sb("tab_lo", [VP, NS, VC * D], F32R)
        onehot = sb("onehot", [VP, PARTS, VH, COLS], F32R)
        xt = sb("xt", [P, PAIR, P, F])
        gram_sb = sb("gram_sb", [P, F, QT])
        z_sb = sb("z_sb", [ZP, ZC, COLS])
        z_hi = sb("z_hi", [ZP, ZC, COLS], F32R)
        z_lo = sb("z_lo", [ZP, ZC, COLS], F32R)
        x_sb = sb("x_sb", [P, COLS])
        x_hi = sb("x_hi", [P, COLS], F32R)
        x_lo = sb("x_lo", [P, COLS], F32R)
        w1z_hi = sb("w1z_hi", [ZP, ZC, C1, P], F32R)
        w1z_lo = sb("w1z_lo", [ZP, ZC, C1, P], F32R)
        w1x_hi = sb("w1x_hi", [P, C1, P], F32R)
        w1x_lo = sb("w1x_lo", [P, C1, P], F32R)
        w2_hi = sb("w2_hi", [P, C1, C2, P], F32R)
        w2_lo = sb("w2_lo", [P, C1, C2, P], F32R)
        w3_sb = sb("w3_sb", [P, C2])
        b1_sb = sb("b1_sb", [P, C1])
        b2_sb = sb("b2_sb", [P, C2])
        h1 = sb("h1", [P, 2, COLS])
        h1_hi = sb("h1_hi", [P, C1, COLS], F32R)
        h1_lo = sb("h1_lo", [P, C1, COLS], F32R)
        h2 = sb("h2", [P, C2, COLS])
        y_sb = sb("y_sb", [1, COLS])
        ones = sb("ones", [P, P])
        ident = sb("ident", [P, P])
        turn_ps = ps("turn_ps", [P, 2, 512])
        select_ps = ps("select_ps", [P, 2, 512])
        gram_ps = ps("gram_ps", [P, 2, 512])
        mlp_ps = ps("mlp_ps", [P, 2, 512])

        small_in = sem("small_in")
        stage_in = [sem("stage_in0"), sem("stage_in1")]
        hi_ready = sem("hi_ready")
        lo_ready = sem("lo_ready")
        w1s_ready = sem("w1s_ready")
        ones_ready = sem("ones_ready")
        ident_ready = sem("ident_ready")
        row_ids_ready = sem("row_ids_ready")
        row_ids_f_ready = sem("row_ids_f_ready")
        gram_cleared = sem("gram_cleared")
        idx_in = [sem(f"idx_in{a}") for a in range(PAIR)]
        dense_in = [sem(f"dense_in{a}") for a in range(PAIR)]
        ids_in = [sem("ids_in_early"), sem("ids_in_late")]
        gathered = [sem(f"gathered{a}") for a in range(PAIR)]
        onehot_ready = sem("onehot_ready")
        onehot_used = sem("onehot_used")
        selected_copied = sem("selected_copied")
        turned = sem("turned")
        turned_copied = sem("turned_copied")
        gram_ready = sem("gram_ready")
        gram_copied = sem("gram_copied")
        z_out = sem("z_out")
        z_in = sem("z_in")
        z_split = sem("z_split")
        x_copied = sem("x_copied")
        x_split = sem("x_split")
        mlp_ready = sem("mlp_ready")
        mlp_copied = sem("mlp_copied")
        h1_hi_ready = sem("h1_hi_ready")
        h1_lo_ready = sem("h1_lo_ready")
        y_out = sem("y_out")

        z_dram = nc.dram_tensor("z_dram", (F * F, NJ, QT), F32, kind="Internal").ap()

        out_v = out.rearrange("(i a j q) o -> i j a (q o)", a=PAIR, j=NJ, q=QUAD)
        ids_v = ids_cols.rearrange("n (i b) -> i n b", b=COLS)
        xt_dense = xt[:, :, :, 0:1].rearrange("d a (j q) f -> d j a (q f)", j=NJ)

        def by_unit(ap, c):
            return ap.rearrange("d (p c) -> d c p", c=c)

        staged = [(selected_tables[k].rearrange("(p c) d -> p (c d)", c=VC), VP, VC * D,
                   tab_hi[:, k, :], tab_lo[:, k, :], None) for k in range(NS)]
        staged += [(w1[D + c * ZP:D + (c + 1) * ZP, :], ZP, N1, w1z_hi[:, c, :, :], w1z_lo[:, c, :, :], C1)
                   for c in range(ZC)]
        staged += [(w2[:, :].rearrange("(p c) n -> p (c n)", c=C1), P, C1 * N2, w2_hi, w2_lo, C2)]

        def staged_view(k):
            _, n, cols, _, _, units = staged[k]
            v = stage[0:n, k % 2, 0:cols]
            if k < NS:
                return v
            if k < NS + ZC:
                return v.rearrange("d (p c) -> d c p", c=units)
            return v.rearrange("d (k p c) -> d k c p", k=C1, c=units)

        NST = len(staged)
        w1s = stage[:, NST % 2, 0:N1]

        block = ctx.enter_context(nc.Block())

        @block.sync
        def _(sp):
            def load_rows(i, a, first):
                if not first:
                    sp.wait_ge(gathered[a], i * (DMA * NG))
                    sp.nop(nofuse=True)
                sp.dma_start(idx[:, a, :], ids_rows[bass.ds(i * COLS + a * P, P), :].bitcast(U32)
                             ).then_inc(idx_in[a], DMA)
                if not first:
                    sp.wait_ge(turned, (i - 1) * (PAIR * GROUPS) + GROUPS * (a + 1))
                    sp.nop(nofuse=True)
                sp.dma_start(rows_sb[:, a, 0, :], dense[bass.ds(i * COLS + a * P, P), :]).then_inc(dense_in[a], DMA)

            def load_ids(i, late, first):
                k0, k1 = (EARLY, NS) if late else (0, EARLY)
                if not first:
                    sp.wait_ge(onehot_ready, (i - 1) * (2 * NS) + 2 * k1)
                    sp.nop(nofuse=True)
                sp.dma_start(ids_sb[:, k0:k1, :], ids_v[bass.ds(i, 1), k0:k1, :].to_broadcast([VP, k1 - k0, COLS])
                             ).then_inc(ids_in[late], DMA)

            def move_z(i, first):
                sp.wait_ge(gram_copied, (i + 1) * (2 * PAIR))
                sp.nop(nofuse=True)
                if not first:
                    sp.wait_ge(z_in, i * (DMA * len(runs)))
                    sp.nop(nofuse=True)
                for j in range(NJ):
                    sp.dma_start(z_dram[:, j, :].rearrange("(f g) q -> f g q", g=F),
                                 gram_sb[j * QUAD:j * QUAD + F, :, :]).then_inc(z_out, DMA)
                sp.wait_ge(z_out, (i + 1) * (DMA * NJ))
                sp.nop(nofuse=True)
                if not first:
                    sp.wait_ge(z_split, i * 2)
                    sp.nop(nofuse=True)
                for e0, n, c, p0 in runs:
                    sp.dma_start(z_sb[p0:p0 + n, c, :],
                                 z_dram[e0:e0 + (n - 1) * (F + 1) + 1:F + 1, :, :].rearrange("e j q -> e (j q)")
                                 ).then_inc(z_in, DMA)

            def store_y(i):
                sp.wait_ge(mlp_copied, (i + 1) * U)
                sp.nop(nofuse=True)
                sp.dma_start(out_v[bass.ds(i, 1)], y_sb[0:1, :].rearrange("o (j a q) -> o j a q", j=NJ, a=PAIR)
                             ).then_inc(y_out, DMA)

            load_rows(0, 0, True)
            load_ids(0, 0, True)
            load_ids(0, 1, True)
            for k, (src, n, cols, _, _, _) in enumerate(staged):
                if k >= 2:
                    sp.wait_ge(lo_ready, k - 1)
                sp.dma_start(stage[0:n, k % 2, 0:cols], src).then_inc(stage_in[k % 2], DMA)
                if k == 0:
                    load_rows(0, 1, True)
            k = NST
            sp.wait_ge(lo_ready, k - 1)
            for h, r0 in enumerate((0, D + NPAIR)):
                sp.dma_start(stage[:, k % 2, h * N1:(h + 1) * N1], w1[r0:r0 + D, :]).then_inc(stage_in[k % 2], DMA)
            sp.dma_start(w3_sb[:, :], w3.rearrange("(p c) o -> p (c o)", c=C2)).then_inc(small_in, DMA)
            sp.dma_start(b1_sb[:, :], b1.rearrange("(p c) -> p c", c=C1)).then_inc(small_in, DMA)
            sp.dma_start(b2_sb[:, :], b2.rearrange("(p c) -> p c", c=C2)).then_inc(small_in, DMA)

            def ahead(i):
                load_ids(i, 0, False)
                load_rows(i, 0, False)
                load_ids(i, 1, False)
                load_rows(i, 1, False)

            ahead(1)
            move_z(0, True)
            ahead(2)
            move_z(1, False)
            with sp.Fori(2, TURNS - 1) as i:
                ahead(i + 1)
                store_y(i - 2)
                move_z(i, False)
            store_y(TURNS - 3)
            move_z(TURNS - 1, False)
            store_y(TURNS - 2)
            store_y(TURNS - 1)
            sp.wait_ge(y_out, TURNS * DMA)

        @block.gpsimd
        def _(gp):
            def gather(i, a, first):
                gp.wait_ge(idx_in[a], (i + 1) * DMA)
                if not first:
                    gp.wait_ge(turned, (i - 1) * (PAIR * GROUPS) + GROUPS * (a + 1))
                    gp.nop(nofuse=True)
                for f in range(NG):
                    gp.indirect_dma_start(
                        out=rows_sb[:, a, f + 1, :], out_offset=None, in_=gathered_tables[f],
                        in_offset=bass.IndirectOffsetOnAxis(ap=idx[:, a, f:f + 1], axis=0)
                    ).then_inc(gathered[a], DMA)

            gp.iota(row_ids[:, :], pattern=[[1, VC]], base=0, channel_multiplier=VC).then_inc(row_ids_ready, 1)
            gp.memset(ones[:, :], 1.0).then_inc(ones_ready, 1)
            gp.wait_ge(ones_ready, 1)
            gp.affine_select(ident[:, :], ones[:, :], pattern=[[-1, P]], compare_op=ALU.is_equal, fill=0.0,
                             base=0, channel_multiplier=1).then_inc(ident_ready, 1)
            for a in range(PAIR):
                gather(0, a, True)
            with gp.Fori(1, TURNS) as i:
                for a in range(PAIR):
                    gather(i, a, False)

        @block.scalar
        def _(act):
            def copy_selected(i, k):
                act.wait_ge(onehot_used, i * (2 * NS) + 2 * k + 2)
                act.copy(xt[:, :, :, R + k:R + k + 1].rearrange("d a p f -> d a (p f)"),
                         select_ps[:, k % 2, 0:COLS].rearrange("d (a p) -> d a p", a=PAIR)
                         ).then_inc(selected_copied, 1)

            def copy_turned(i, a, first):
                if a == 0 and not first:
                    act.wait_ge(x_copied, i)
                for g in range(GROUPS):
                    n = min(GROUP, R - g * GROUP)
                    act.wait_ge(turned, i * (PAIR * GROUPS) + a * GROUPS + g + 1)
                    act.copy(xt[:, a, :, g * GROUP:g * GROUP + n].rearrange("d p f -> d f p"),
                             turn_ps[:, (a * GROUPS + g) % 2, 0:n * P].rearrange("d (f p) -> d f p", p=P)
                             ).then_inc(turned_copied, 1)

            def layer1(i, u, first):
                act.wait_ge(mlp_ready, i * U + u + 1)
                if not (first and u < 2):
                    act.wait_ge(h1_lo_ready, i * C1 + u - 1)
                act.activation(h1[:, u % 2, :], mlp_ps[:, u % 2, 0:COLS], ACT.Relu, bias=b1_sb[:, u:u + 1]
                               ).then_inc(mlp_copied, 1)
                act.wait_ge(mlp_copied, i * U + u + 1)
                act.copy(h1_hi[:, u, :], h1[:, u % 2, :]).then_inc(h1_hi_ready, 1)

            def layer2(i, c):
                act.wait_ge(mlp_ready, i * U + C1 + c + 1)
                act.activation(h2[:, c, :], mlp_ps[:, (C1 + c) % 2, 0:COLS], ACT.Relu, bias=b2_sb[:, c:c + 1]
                               ).then_inc(mlp_copied, 1)

            def result(i, first):
                act.wait_ge(mlp_ready, (i + 1) * U)
                if not first:
                    act.wait_ge(y_out, i * DMA)
                act.copy(y_sb[0:1, :], mlp_ps[0:1, (U - 1) % 2, 0:COLS]).then_inc(mlp_copied, 1)

            def pair(i, first):
                for k in range(NS):
                    copy_selected(i, k)
                    if k == EARLY - 1:
                        copy_turned(i, 0, False)
                    if EARLY <= k < EARLY + C1:
                        layer1(i - 2, k - EARLY, first)
                    if EARLY + C1 <= k < EARLY + C1 + C2:
                        layer2(i - 2, k - EARLY - C1)
                copy_turned(i, 1, False)
                result(i - 2, first)

            def mlp(i):
                for u in range(C1):
                    layer1(i, u, False)
                for c in range(C2):
                    layer2(i, c)
                result(i, False)

            def split_hi(k):
                act.wait_ge(stage_in[k % 2], (k // 2 + 1) * DMA)
                act.copy(staged[k][3][:], staged_view(k)).then_inc(hi_ready, 1)

            for k in range(NST):
                split_hi(k)
                if 1 <= k <= NS:
                    copy_selected(0, k - 1)
            act.wait_ge(w1s_ready, 1)
            act.copy(w1x_hi[:, :, :], by_unit(w1s, C1)).then_inc(hi_ready, 1)
            act.wait_ge(small_in, 3 * DMA)
            copy_turned(0, 0, True)
            copy_turned(0, 1, True)
            for k in range(NS):
                copy_selected(1, k)
                if k == EARLY - 1:
                    copy_turned(1, 0, False)
            copy_turned(1, 1, False)
            pair(2, True)
            with act.Fori(3, TURNS) as i:
                pair(i, False)
            mlp(TURNS - 2)
            mlp(TURNS - 1)

        @block.vector
        def _(dve):
            def split_lo(k):
                dve.wait_ge(hi_ready, k + 1)
                dve.tensor_tensor(staged[k][4][:], staged_view(k), staged[k][3][:].bitcast(F32), ALU.subtract
                                  ).then_inc(lo_ready, 1)

            def make_onehot(i, n, first):
                k, h = n // 2, n % 2
                if h == 0 and k in (0, EARLY):
                    dve.wait_ge(ids_in[k // EARLY], (i + 1) * DMA)
                if not (first and n < PARTS):
                    dve.wait_ge(onehot_used, i * (2 * NS) + n + 1 - PARTS)
                for c in range(VH):
                    ins = dve.tensor_scalar(onehot[:, n % PARTS, c, :], ids_sb[:, k, :],
                                            row_ids_f[:, h * VH + c:h * VH + c + 1], None, ALU.is_equal)
                ins.then_inc(onehot_ready, 1)

            def copy_grams(i, a, first):
                if a == 0 and not first:
                    dve.wait_ge(z_out, i * (DMA * NJ))
                for b in range(2):
                    dve.wait_ge(gram_ready, i * (2 * PAIR) + 2 * a + b + 1)
                    q0 = a * QUAD + b * HALF
                    dve.tensor_copy(gram_sb[:, :, q0:q0 + HALF],
                                    gram_ps[:, b, 0:HALF * F].rearrange("p (q g) -> p g q", g=F)
                                    ).then_inc(gram_copied, 1)

            def copy_x(i, first):
                dve.wait_ge(turned_copied, (i + 1) * (PAIR * GROUPS))
                if not first:
                    dve.wait_ge(x_split, i * 2)
                dve.tensor_copy(x_sb[:, :].rearrange("d (j a q) -> d j a q", j=NJ, a=PAIR), xt_dense
                                ).then_inc(x_copied, 1)

            def split(i, first):
                dve.wait_ge(z_in, (i + 1) * (DMA * len(runs)))
                dve.wait_ge(x_copied, i + 1)
                if not first:
                    dve.wait_ge(mlp_ready, (i - 1) * U + C1)
                dve.tensor_copy(z_hi[:, :, :], z_sb[:, :, :]).then_inc(z_split, 1)
                dve.tensor_copy(x_hi[:, :], x_sb[:, :]).then_inc(x_split, 1)
                dve.wait_ge(z_split, 2 * i + 1)
                dve.tensor_tensor(z_lo[:, :, :], z_sb[:, :, :], z_hi[:, :, :].bitcast(F32), ALU.subtract
                                  ).then_inc(z_split, 1)
                dve.wait_ge(x_split, 2 * i + 1)
                dve.tensor_tensor(x_lo[:, :], x_sb[:, :], x_hi[:, :].bitcast(F32), ALU.subtract
                                  ).then_inc(x_split, 1)

            def split_h1(i, u):
                dve.wait_ge(h1_hi_ready, i * C1 + u + 1)
                dve.tensor_tensor(h1_lo[:, u, :], h1[:, u % 2, :], h1_hi[:, u, :].bitcast(F32), ALU.subtract
                                  ).then_inc(h1_lo_ready, 1)

            def pair(i, first, last):
                for n in range(PARTS, 2 * NS):
                    make_onehot(i, n, False)
                    if n % 2 and EARLY < n // 2 <= EARLY + C1 and not first:
                        split_h1(i - 2, n // 2 - EARLY - 1)
                split(i - 1, first)
                if not last:
                    for n in range(PARTS):
                        make_onehot(i + 1, n, False)
                copy_grams(i, 0, False)
                copy_grams(i, 1, False)
                copy_x(i, False)

            for b in range(2):
                dve.memset(gram_ps[:, b, 0:HALF * F], 0.0).then_inc(gram_cleared, 1)
            dve.wait_ge(row_ids_ready, 1)
            dve.tensor_copy(row_ids_f[:, :], row_ids[:, :]).then_inc(row_ids_f_ready, 1)
            dve.wait_ge(row_ids_f_ready, 1)
            for k in range(NS):
                split_lo(k)
                for h in range(2):
                    make_onehot(0, 2 * k + h, True)
            for k in range(NS, NST):
                split_lo(k)
            dve.wait_ge(stage_in[NST % 2], (NST // 2 + 2) * DMA)
            dve.tensor_tensor(w1s, w1s, stage[:, NST % 2, N1:2 * N1], ALU.add
                              ).then_inc(w1s_ready, 1)
            dve.wait_ge(hi_ready, NST + 1)
            dve.tensor_tensor(w1x_lo[:, :, :], by_unit(w1s, C1), w1x_hi[:, :, :].bitcast(F32), ALU.subtract
                              ).then_inc(lo_ready, 1)
            for n in range(PARTS):
                make_onehot(1, n, False)
            copy_grams(0, 0, True)
            copy_grams(0, 1, True)
            copy_x(0, True)
            pair(1, True, False)
            with dve.Fori(2, TURNS - 1) as i:
                pair(i, False, False)
            pair(TURNS - 1, False, True)
            for u in range(C1):
                split_h1(TURNS - 2, u)
            split(TURNS - 1, False)
            for u in range(C1):
                split_h1(TURNS - 1, u)

        @block.tensor
        def _(pe):
            def select(i, k, first):
                if first:
                    pe.wait_ge(lo_ready, k + 1)
                if not (first and k < 2):
                    pe.wait_ge(selected_copied, i * NS + max(k - 1, 0))
                for h in range(2):
                    n = 2 * k + h
                    pe.wait_ge(onehot_ready, i * (2 * NS) + n + 1)
                    for c in range(VH):
                        for tab in (tab_hi, tab_lo):
                            c0 = (h * VH + c) * D
                            mm = pe.matmul(select_ps[:, k % 2, 0:COLS], tab[:, k, c0:c0 + D],
                                           onehot[:, n % PARTS, c, :],
                                           start=(c0 == 0 and tab is tab_hi),
                                           stop=(c0 == (VC - 1) * D and tab is tab_lo))
                    mm.then_inc(onehot_used, 1)

            def turn(i, a, first):
                pe.wait_ge(gathered[a], (i + 1) * (DMA * NG))
                pe.wait_ge(dense_in[a], (i + 1) * DMA)
                for g in range(GROUPS):
                    k = a * GROUPS + g
                    if not (first and k < 2):
                        pe.wait_ge(turned_copied, i * (PAIR * GROUPS) + k - 1)
                    n = min(GROUP, R - g * GROUP)
                    for m in range(n):
                        mm = pe.transpose(turn_ps[:, k % 2, m * P:(m + 1) * P],
                                          rows_sb[:, a, g * GROUP + m, :], ident[:, :])
                    mm.then_inc(turned, 1)

            def grams(i, a, first):
                pe.wait_ge(turned_copied, i * (PAIR * GROUPS) + (a + 1) * GROUPS)
                pe.wait_ge(selected_copied, (i + 1) * NS)
                for b in range(2):
                    if not (first and a == 0):
                        pe.wait_ge(gram_copied, i * (2 * PAIR) + 2 * a + b - 1)
                    for q in range(HALF):
                        for j in range(NJ):
                            p = j * QUAD + b * HALF + q
                            mm = pe.matmul(gram_ps[j * QUAD:j * QUAD + F, b, q * F:(q + 1) * F],
                                           xt[:, a, p, :], xt[:, a, p, :], start=True, stop=True,
                                           tile_position=(0, j * QUAD))
                    mm.then_inc(gram_ready, 1)

            def layer1(i, u, first):
                if u == 0:
                    pe.wait_ge(z_split, (i + 1) * 2)
                    pe.wait_ge(x_split, (i + 1) * 2)
                if not (first and u < 2):
                    pe.wait_ge(mlp_copied, i * U + max(u - 1, 0))
                o = mlp_ps[:, u % 2, 0:COLS]
                for c in range(ZC):
                    for n, (w, z) in enumerate(((w1z_hi, z_hi), (w1z_hi, z_lo), (w1z_lo, z_hi))):
                        pe.matmul(o, w[:, c, u, :], z[:, c, :], start=(c == 0 and n == 0), stop=False)
                for n, (w, x) in enumerate(((w1x_hi, x_hi), (w1x_hi, x_lo), (w1x_lo, x_hi))):
                    mm = pe.matmul(o, w[:, u, :], x[:, :], start=False, stop=(n == 2))
                mm.then_inc(mlp_ready, 1)

            def layer2(i, m):
                if m == 0:
                    pe.wait_ge(h1_lo_ready, (i + 1) * C1)
                u = C1 + m
                pe.wait_ge(mlp_copied, i * U + u - 1)
                for c in range(C1):
                    for n, (w, h) in enumerate(((w2_hi, h1_hi), (w2_hi, h1_lo), (w2_lo, h1_hi))):
                        mm = pe.matmul(mlp_ps[:, u % 2, 0:COLS], w[:, c, m, :], h[:, c, :],
                                       start=(c == 0 and n == 0), stop=(c == C1 - 1 and n == 2))
                mm.then_inc(mlp_ready, 1)

            def result(i):
                pe.wait_ge(mlp_copied, i * U + U - 1)
                for c in range(C2):
                    mm = pe.matmul(mlp_ps[0:1, (U - 1) % 2, 0:COLS], w3_sb[:, c:c + 1], h2[:, c, :],
                                   start=(c == 0), stop=(c == C2 - 1))
                mm.then_inc(mlp_ready, 1)

            def pair(i, first):
                for k in range(NS):
                    select(i, k, False)
                    if k == EARLY - 1:
                        turn(i, 0, False)
                    if EARLY <= k < EARLY + C1:
                        layer1(i - 2, k - EARLY, first)
                    if EARLY + C1 <= k < EARLY + C1 + C2:
                        layer2(i - 2, k - EARLY - C1)
                grams(i, 0, False)
                turn(i, 1, False)
                result(i - 2)
                grams(i, 1, False)

            def mlp(i):
                for u in range(C1):
                    layer1(i, u, False)
                for m in range(C2):
                    layer2(i, m)
                result(i)

            pe.wait_ge(ident_ready, 1)
            pe.wait_ge(gram_cleared, 2)
            for k in range(NS):
                select(0, k, True)
            turn(0, 0, True)
            grams(0, 0, True)
            turn(0, 1, True)
            grams(0, 1, True)
            for k in range(NS):
                select(1, k, False)
                if k == EARLY - 1:
                    turn(1, 0, False)
            grams(1, 0, False)
            turn(1, 1, False)
            grams(1, 1, False)
            pe.wait_ge(lo_ready, NST + 1)
            pe.wait_ge(small_in, 3 * DMA)
            pair(2, True)
            with pe.Fori(3, TURNS) as i:
                pair(i, False)
            mlp(TURNS - 2)
            mlp(TURNS - 1)


def kernel(**inputs):
    import numpy as np
    import concourse.bacc as bacc
    from concourse.bass_utils import run_bass_kernel_spmd as run

    B, NT = inputs["ids"].shape
    D = inputs["r_dense_features"].shape[1]
    rows, chosen = feature_order([inputs[f"tbl_{t}"].shape[0] for t in range(NT)])
    feature = [0] + [t + 1 for t in rows + chosen]
    F = NT + 1
    where = {}
    for a in range(F):
        for b in range(a + 1, F):
            where[a, b] = D + len(where)
    _, pairs = pair_order(F)
    order = [where[min(feature[a], feature[b]), max(feature[a], feature[b])] for a, b in pairs]
    w1 = inputs["W_top1"]
    order = list(range(D)) + order + list(range(D + len(order), w1.shape[0]))

    ids = np.asarray(inputs["ids"])
    given = {"dense": inputs["r_dense_features"], "ids_rows": ids[:, rows], "ids_cols": ids[:, chosen].T,
             "w1": np.asarray(w1)[order], "b1": inputs["b_top1"], "w2": inputs["W_top2"],
             "b2": inputs["b_top2"], "w3": inputs["W_top3"]}
    given.update({f"tbl_{t}": inputs[f"tbl_{t}"] for t in range(NT)})
    nc = bacc.Bacc("TRN2", target_bir_lowering=False, num_devices=1)
    arrays, aps = {}, {}
    for name, a in given.items():
        a = np.ascontiguousarray(a)
        arrays["in_" + name] = a
        aps[name] = nc.dram_tensor("in_" + name, a.shape, mybir.dt.from_np(a.dtype), kind="ExternalInput").ap()
    out = nc.dram_tensor("out", (B, 1), F32, kind="ExternalOutput").ap()
    build_dlrm(nc, aps["dense"], aps["ids_rows"], aps["ids_cols"], [aps[f"tbl_{t}"] for t in rows],
               [aps[f"tbl_{t}"] for t in chosen], aps["w1"], aps["b1"], aps["w2"], aps["b2"], aps["w3"], out)
    r = run(nc, [arrays], core_ids=[0])
    return r.results[0]["out"]
```

```python
from contextlib import ExitStack

import concourse.bass as bass
from concourse import mybir

P = 128
F32 = mybir.dt.float32
F32R = mybir.dt.float32r
I32 = mybir.dt.int32
U32 = mybir.dt.uint32
ALU = mybir.AluOpType
ACT = mybir.ActivationFunctionType

SELECTED = 9
QUAD = 32
NJ = P // QUAD
PAIR = 2
GROUP = 4
EARLY = 3
PARTS = 6
DMA = 16

TURNED_BY = [1, 2, 3, 3, 4, 5, 6, 7, 8]
LAYER1_AFTER = {1: 0, 2: 1, 3: 2, 4: 3}
LAYER2_AFTER = {6: 0, 8: 1}
WEIGHTS_AFTER = {0: 1, 2: 2, 3: 3, 8: 4}


def feature_order(sizes):
    least = min(sizes)
    chosen = [t for t, v in enumerate(sizes) if v == least][:SELECTED]
    return [t for t in range(len(sizes)) if t not in chosen], chosen


def pair_order(F):
    blocks, pairs = [], []
    for k in range(1, (F + 1) // 2 + 1):
        f0 = F // 2 if k == (F + 1) // 2 else 0
        blocks.append(((F + 1) * f0 + k, F - 1 - f0))
        for f in range(f0, F - 1):
            a, b = divmod((F + 1) * f + k, F)
            pairs.append((min(a, b), max(a, b)))
    assert F % 2 == 1 and len(set(pairs)) == len(pairs) == F * (F - 1) // 2
    return blocks, pairs


def build_dlrm(nc, dense, ids_rows, ids_cols, gathered_tables, selected_tables, w1, b1, w2, b2, w3, out):
    B, D = dense.shape
    NG, NS = len(gathered_tables), len(selected_tables)
    R = 1 + NG
    F = R + NS
    N1, N2 = w1.shape[1], w2.shape[1]
    C1, C2 = N1 // P, N2 // P
    NPAIR = F * (F - 1) // 2
    COLS = PAIR * P
    TURNS = B // COLS
    QT = QUAD * PAIR
    HALF = QUAD // 2
    GROUPS = -(-R // GROUP)
    V = selected_tables[0].shape[0]
    VC = -(-V // P)
    VP = V // VC
    VH = VC // 2
    ZC = -(-NPAIR // P)
    ZP = NPAIR // ZC
    U = C1 + C2 + 1
    assert len(TURNED_BY) == NS and TURNED_BY[-1] < PAIR * GROUPS
    assert D == P and B == TURNS * COLS and V == VC * VP and VC == 2 * VH and 2 * NS % PARTS == 0 and NPAIR == ZC * ZP

    runs, at = [], 0
    for e0, n in pair_order(F)[0]:
        while n:
            m = min(n, ZP - at % ZP)
            last = runs[-1] if runs else None
            if last and m == last[2] and e0 == last[0] + last[1] and at % ZP:
                last[1] += 1
            else:
                runs.append([e0, 1, m, at // ZP, at % ZP])
            e0, n, at = e0 + m * (F + 1), n - m, at + m
    chunk_runs = [sum(r[3] == c for r in runs) for c in range(ZC)]

    with ExitStack() as ctx:
        def sb(name, shape, dt=F32):
            return ctx.enter_context(nc.sbuf_tensor(name, shape, dt))

        def ps(name, shape):
            return ctx.enter_context(nc.psum_tensor(name, shape, F32))

        def sem(name):
            return ctx.enter_context(nc.semaphore(name))

        idx = sb("idx", [P, PAIR, NG], U32)
        rows_sb = sb("rows_sb", [P, PAIR, R, D])
        ids_sb = sb("ids_sb", [VP, NS, COLS], I32)
        row_ids = sb("row_ids", [VP, VC], I32)
        row_ids_f = sb("row_ids_f", [VP, VC])
        stage = sb("stage", [P, 2, VC * D])
        late = sb("late", [P, ZC + 1 + 2 + C2, COLS])
        z_sb = late[0:ZP, 0:ZC, :]
        x_sb = late[:, ZC, :]
        h1 = late[:, ZC + 1:ZC + 3, :]
        h2 = late[:, ZC + 3:ZC + 3 + C2, :]
        tab_hi = sb("tab_hi", [VP, NS, VC * D], F32R)
        tab_lo = sb("tab_lo", [VP, NS, VC * D], F32R)
        onehot_all = sb("onehot", [P, PARTS, VH, COLS], F32R)
        onehot = onehot_all[0:VP, :, :, :]
        xt = sb("xt", [P, PAIR, P, F])
        gram_sb = sb("gram_sb", [P, F, QT])
        z_hi = sb("z_hi", [ZP, ZC, COLS], F32R)
        z_lo = sb("z_lo", [ZP, ZC, COLS], F32R)
        x_hi = sb("x_hi", [P, COLS], F32R)
        x_lo = sb("x_lo", [P, COLS], F32R)
        w1z_hi = sb("w1z_hi", [ZP, ZC, C1, P], F32R)
        w1z_lo = sb("w1z_lo", [ZP, ZC, C1, P], F32R)
        w1x_hi = sb("w1x_hi", [P, C1, P], F32R)
        w1x_lo = sb("w1x_lo", [P, C1, P], F32R)
        w2_hi = sb("w2_hi", [P, C1, C2, P], F32R)
        w2_lo = sb("w2_lo", [P, C1, C2, P], F32R)
        w3_sb = sb("w3_sb", [P, C2])
        b1_sb = sb("b1_sb", [P, C1])
        b2_sb = sb("b2_sb", [P, C2])
        h1_hi = sb("h1_hi", [P, C1, COLS], F32R)
        h1_lo = sb("h1_lo", [P, C1, COLS], F32R)
        y_sb = sb("y_sb", [1, COLS])
        ones = sb("ones", [P, P])
        ident = sb("ident", [P, P])
        turn_ps = ps("turn_ps", [P, 2, 512])
        select_ps = ps("select_ps", [P, 2, 512])
        gram_ps = ps("gram_ps", [P, 2, 512])
        mlp_ps = ps("mlp_ps", [P, 2, 512])

        small_in = sem("small_in")
        stage_in = [sem("stage_in0"), sem("stage_in1")]
        hi_ready = sem("hi_ready")
        lo_ready = sem("lo_ready")
        w1s_ready = sem("w1s_ready")
        ones_ready = sem("ones_ready")
        ident_ready = sem("ident_ready")
        row_ids_ready = sem("row_ids_ready")
        row_ids_f_ready = sem("row_ids_f_ready")
        gram_cleared = sem("gram_cleared")
        idx_in = [sem(f"idx_in{a}") for a in range(PAIR)]
        dense_in = [sem(f"dense_in{a}") for a in range(PAIR)]
        ids_in = [sem("ids_in_early"), sem("ids_in_late")]
        gathered = [[sem(f"gathered{a}_{g}") for g in range(GROUPS)] for a in range(PAIR)]
        onehot_ready = sem("onehot_ready")
        onehot_used = sem("onehot_used")
        selected_copied = sem("selected_copied")
        turned = sem("turned")
        turned_copied = sem("turned_copied")
        gram_ready = sem("gram_ready")
        gram_copied = sem("gram_copied")
        z_out = sem("z_out")
        z_in = [sem(f"z_in{c}") for c in range(ZC)]
        z_split = sem("z_split")
        x_copied = sem("x_copied")
        x_split = sem("x_split")
        mlp_ready = sem("mlp_ready")
        mlp_copied = sem("mlp_copied")
        last_ready = sem("last_ready")
        last_copied = sem("last_copied")
        h1_hi_ready = sem("h1_hi_ready")
        h1_lo_ready = sem("h1_lo_ready")
        y_out = sem("y_out")

        z_dram = nc.dram_tensor("z_dram", (F * F, NJ, QT), F32, kind="Internal").ap()

        out_v = out.rearrange("(i a j q) o -> i j a (q o)", a=PAIR, j=NJ, q=QUAD)
        ids_v = ids_cols.rearrange("n (i b) -> i n b", b=COLS)
        xt_dense = xt[:, :, :, 0:1].rearrange("d a (j q) f -> d j a (q f)", j=NJ)

        def by_unit(ap, c):
            return ap.rearrange("d (p c) -> d c p", c=c)

        staged = [(selected_tables[k].rearrange("(p c) d -> p (c d)", c=VC), VP, VC * D,
                   tab_hi[:, k, :], tab_lo[:, k, :], None) for k in range(NS)]
        staged += [(w1[D + c * ZP:D + (c + 1) * ZP, :], ZP, N1, w1z_hi[:, c, :, :], w1z_lo[:, c, :, :], C1)
                   for c in range(ZC)]
        staged += [(w2[:, :].rearrange("(p c) n -> p (c n)", c=C1), P, C1 * N2, w2_hi, w2_lo, C2)]

        def staged_view(k):
            _, n, cols, _, _, units = staged[k]
            v = stage[0:n, k % 2, 0:cols]
            if k < NS:
                return v
            if k < NS + ZC:
                return v.rearrange("d (p c) -> d c p", c=units)
            return v.rearrange("d (k p c) -> d k c p", k=C1, c=units)

        NST = len(staged)
        w1s = stage[:, NST % 2, 0:N1]

        last_x_hi = onehot_all[:, 0, 0, :]
        last_x_lo = onehot_all[:, 0, 1, :]
        last_banks = [select_ps[:, 0, :], select_ps[:, 1, :], turn_ps[:, 0, :], turn_ps[:, 1, :]]
        assert len(last_banks) == C1

        block = ctx.enter_context(nc.Block())

        @block.sync
        def _(sp):
            def load_rows(i, a, first):
                if not first:
                    sp.wait_ge(turned, (i - 1) * (PAIR * GROUPS) + GROUPS * (a + 1))
                    sp.nop(nofuse=True)
                sp.dma_start(idx[:, a, :], ids_rows[bass.ds(i * COLS + a * P, P), :].bitcast(U32)
                             ).then_inc(idx_in[a], DMA)
                sp.dma_start(rows_sb[:, a, 0, :], dense[bass.ds(i * COLS + a * P, P), :]).then_inc(dense_in[a], DMA)

            def load_ids(i, late, first):
                k0, k1 = (EARLY, NS) if late else (0, EARLY)
                if not first:
                    sp.wait_ge(onehot_ready, (i - 1) * (2 * NS) + 2 * k1)
                    sp.nop(nofuse=True)
                sp.dma_start(ids_sb[:, k0:k1, :], ids_v[bass.ds(i, 1), k0:k1, :].to_broadcast([VP, k1 - k0, COLS])
                             ).then_inc(ids_in[late], DMA)

            def write_z(i, first):
                sp.wait_ge(gram_copied, (i + 1) * (2 * PAIR))
                sp.nop(nofuse=True)
                if not first:
                    for c in range(ZC):
                        sp.wait_ge(z_in[c], i * (DMA * chunk_runs[c]))
                        sp.nop(nofuse=True)
                for j in range(NJ):
                    sp.dma_start(z_dram[:, j, :].rearrange("(f g) q -> f g q", g=F),
                                 gram_sb[j * QUAD:j * QUAD + F, :, :]).then_inc(z_out, DMA)

            def read_z(i, first):
                sp.wait_ge(z_out, (i + 1) * (DMA * NJ))
                sp.nop(nofuse=True)
                if not first:
                    sp.wait_ge(z_split, i * 2)
                    sp.nop(nofuse=True)
                for e0, m, n, c, p0 in runs:
                    sp.dma_start(z_sb[p0:p0 + m * n, c, :],
                                 bass.AP(tensor=z_dram.tensor, offset=z_dram.offset + e0 * COLS,
                                         ap=[[COLS, m], [(F + 1) * COLS, n], [1, COLS]])
                                 ).then_inc(z_in[c], DMA)

            def store_y(i, last=False):
                if last:
                    sp.wait_ge(last_copied, U)
                else:
                    sp.wait_ge(mlp_copied, (i + 1) * U)
                    sp.nop(nofuse=True)
                sp.dma_start(out_v[bass.ds(i, 1)], y_sb[0:1, :].rearrange("o (j a q) -> o j a q", j=NJ, a=PAIR)
                             ).then_inc(y_out, DMA)

            def load_staged(k):
                if k >= 2:
                    sp.wait_ge(lo_ready, k - 1)
                src, n, cols = staged[k][:3]
                sp.dma_start(stage[0:n, k % 2, 0:cols], src).then_inc(stage_in[k % 2], DMA)

            def ahead(i):
                load_ids(i, 0, False)
                load_rows(i, 0, False)
                load_ids(i, 1, False)
                load_rows(i, 1, False)

            load_rows(0, 0, True)
            load_staged(0)
            load_ids(0, 0, True)
            load_staged(1)
            load_ids(0, 1, True)
            load_rows(0, 1, True)
            for k in range(2, NS):
                load_staged(k)
            load_ids(1, 0, False)
            load_rows(1, 0, False)
            for k in range(NS, NS + 2):
                load_staged(k)
            sp.dma_start(w3_sb[:, :], w3.rearrange("(p c) o -> p (c o)", c=C2)).then_inc(small_in, DMA)
            sp.dma_start(b1_sb[:, :], b1.rearrange("(p c) -> p c", c=C1)).then_inc(small_in, DMA)
            sp.dma_start(b2_sb[:, :], b2.rearrange("(p c) -> p c", c=C2)).then_inc(small_in, DMA)
            load_ids(1, 1, False)
            load_rows(1, 1, False)
            write_z(0, True)
            for k in range(NS + 2, NST):
                load_staged(k)
            read_z(0, True)
            load_ids(2, 0, False)
            load_rows(2, 0, False)
            sp.wait_ge(lo_ready, NST - 1)
            for h, r0 in enumerate((0, D + NPAIR)):
                sp.dma_start(stage[:, NST % 2, h * N1:(h + 1) * N1], w1[r0:r0 + D, :]).then_inc(stage_in[NST % 2], DMA)
            load_ids(2, 1, False)
            load_rows(2, 1, False)
            write_z(1, False)
            read_z(1, False)
            with sp.Fori(2, TURNS - 1) as i:
                ahead(i + 1)
                store_y(i - 2)
                write_z(i, False)
                read_z(i, False)
            store_y(TURNS - 3)
            write_z(TURNS - 1, False)
            read_z(TURNS - 1, False)
            store_y(TURNS - 2)
            store_y(TURNS - 1, True)
            sp.wait_ge(y_out, TURNS * DMA)

        @block.gpsimd
        def _(gp):
            def gather(i, a, first):
                gp.wait_ge(idx_in[a], (i + 1) * DMA)
                for g in range(GROUPS):
                    if not first:
                        gp.wait_ge(turned, (i - 1) * (PAIR * GROUPS) + a * GROUPS + g + 1)
                        gp.nop(nofuse=True)
                    for f in range(max(g * GROUP, 1), min((g + 1) * GROUP, R)):
                        gp.indirect_dma_start(
                            out=rows_sb[:, a, f, :], out_offset=None, in_=gathered_tables[f - 1],
                            in_offset=bass.IndirectOffsetOnAxis(ap=idx[:, a, f - 1:f], axis=0)
                        ).then_inc(gathered[a][g], DMA)

            gp.iota(row_ids[:, :], pattern=[[1, VC]], base=0, channel_multiplier=VC).then_inc(row_ids_ready, 1)
            gp.memset(ones[:, :], 1.0).then_inc(ones_ready, 1)
            gp.wait_ge(ones_ready, 1)
            gp.affine_select(ident[:, :], ones[:, :], pattern=[[-1, P]], compare_op=ALU.is_equal, fill=0.0,
                             base=0, channel_multiplier=1).then_inc(ident_ready, 1)
            for a in range(PAIR):
                gather(0, a, True)
            with gp.Fori(1, TURNS) as i:
                for a in range(PAIR):
                    gather(i, a, False)

        @block.scalar
        def _(act):
            def copy_selected(i, k):
                act.wait_ge(onehot_used, i * (2 * NS) + 2 * k + 2)
                act.copy(xt[:, :, :, R + k:R + k + 1].rearrange("d a p f -> d a (p f)"),
                         select_ps[:, k % 2, 0:COLS].rearrange("d (a p) -> d a p", a=PAIR)
                         ).then_inc(selected_copied, 1)

            def copy_turned(i, t, first):
                a, g = t // GROUPS, t % GROUPS
                if t == 0 and not first:
                    act.wait_ge(x_copied, i)
                n = min(GROUP, R - g * GROUP)
                act.wait_ge(turned, i * (PAIR * GROUPS) + t + 1)
                act.copy(xt[:, a, :, g * GROUP:g * GROUP + n].rearrange("d p f -> d f p"),
                         turn_ps[:, t % 2, 0:n * P].rearrange("d (f p) -> d f p", p=P)).then_inc(turned_copied, 1)

            def layer1(i, u, first):
                act.wait_ge(mlp_ready, i * U + u + 1)
                if not (first and u < 2):
                    act.wait_ge(h1_lo_ready, i * C1 + u - 1)
                act.activation(h1[:, u % 2, :], mlp_ps[:, u % 2, 0:COLS], ACT.Relu, bias=b1_sb[:, u:u + 1]
                               ).then_inc(mlp_copied, 1)
                act.wait_ge(mlp_copied, i * U + u + 1)
                act.copy(h1_hi[:, u, :], h1[:, u % 2, :]).then_inc(h1_hi_ready, 1)

            def layer2(i, c):
                act.wait_ge(mlp_ready, i * U + C1 + c + 1)
                act.activation(h2[:, c, :], mlp_ps[:, (C1 + c) % 2, 0:COLS], ACT.Relu, bias=b2_sb[:, c:c + 1]
                               ).then_inc(mlp_copied, 1)

            def result(i, first):
                act.wait_ge(mlp_ready, (i + 1) * U)
                if not first:
                    act.wait_ge(y_out, i * DMA)
                act.copy(y_sb[0:1, :], mlp_ps[0:1, (U - 1) % 2, 0:COLS]).then_inc(mlp_copied, 1)

            def pair(i, first, mlp, first_mlp):
                done = 0
                for k in range(NS):
                    if first:
                        split_hi(k + 1)
                    copy_selected(i, k)
                    if not first and not mlp and k in WEIGHTS_AFTER:
                        split_weights(WEIGHTS_AFTER[k])
                    for t in range(done, TURNED_BY[k]):
                        copy_turned(i, t, first)
                    done = TURNED_BY[k]
                    if mlp and k in LAYER1_AFTER:
                        layer1(i - 2, LAYER1_AFTER[k], first_mlp)
                    if mlp and k in LAYER2_AFTER:
                        layer2(i - 2, LAYER2_AFTER[k])
                for t in range(done, PAIR * GROUPS):
                    copy_turned(i, t, first)
                if mlp:
                    result(i - 2, first_mlp)

            def last_layer1(i, u):
                act.wait_ge(last_ready, u + 1)
                act.wait_ge(h1_lo_ready, i * C1 + u - 1)
                act.activation(h1[:, u % 2, :], last_banks[u][:, 0:COLS], ACT.Relu, bias=b1_sb[:, u:u + 1]
                               ).then_inc(last_copied, 1)
                act.wait_ge(last_copied, u + 1)
                act.copy(h1_hi[:, u, :], h1[:, u % 2, :]).then_inc(h1_hi_ready, 1)

            def last_layer2(c):
                act.wait_ge(last_ready, C1 + c + 1)
                act.activation(h2[:, c, :], gram_ps[:, c, 0:COLS], ACT.Relu, bias=b2_sb[:, c:c + 1]
                               ).then_inc(last_copied, 1)

            def last_result(i):
                act.wait_ge(last_ready, U)
                act.wait_ge(y_out, i * DMA)
                act.copy(y_sb[0:1, :], mlp_ps[0:1, 1, 0:COLS]).then_inc(last_copied, 1)

            def split_hi(k):
                act.wait_ge(stage_in[k % 2], (k // 2 + 1) * DMA)
                act.copy(staged[k][3][:], staged_view(k)).then_inc(hi_ready, 1)

            def split_weights(m):
                if NS + m < NST:
                    split_hi(NS + m)
                else:
                    act.wait_ge(w1s_ready, 1)
                    act.copy(w1x_hi[:, :, :], by_unit(w1s, C1)).then_inc(hi_ready, 1)

            split_hi(0)
            pair(0, True, False, False)
            pair(1, False, False, False)
            act.wait_ge(small_in, 3 * DMA)
            pair(2, False, True, True)
            with act.Fori(3, TURNS) as i:
                pair(i, False, True, False)
            for u in range(C1):
                layer1(TURNS - 2, u, False)
            for c in range(C2):
                layer2(TURNS - 2, c)
            result(TURNS - 2, False)
            for u in range(C1):
                last_layer1(TURNS - 1, u)
            for c in range(C2):
                last_layer2(c)
            last_result(TURNS - 1)

        @block.vector
        def _(dve):
            def split_lo(k):
                dve.wait_ge(hi_ready, k + 1)
                dve.tensor_tensor(staged[k][4][:], staged_view(k), staged[k][3][:].bitcast(F32), ALU.subtract
                                  ).then_inc(lo_ready, 1)

            def make_onehot(i, n, first):
                k, h = n // 2, n % 2
                if h == 0 and k in (0, EARLY):
                    dve.wait_ge(ids_in[k // EARLY], (i + 1) * DMA)
                if not (first and n < PARTS):
                    dve.wait_ge(onehot_used, i * (2 * NS) + n + 1 - PARTS)
                for c in range(VH):
                    ins = dve.tensor_scalar(onehot[:, n % PARTS, c, :], ids_sb[:, k, :],
                                            row_ids_f[:, h * VH + c:h * VH + c + 1], None, ALU.is_equal)
                ins.then_inc(onehot_ready, 1)

            def copy_grams(i, a, first):
                if a == 0 and not first:
                    dve.wait_ge(z_out, i * (DMA * NJ))
                for b in range(2):
                    dve.wait_ge(gram_ready, i * (2 * PAIR) + 2 * a + b + 1)
                    q0 = a * QUAD + b * HALF
                    dve.tensor_copy(gram_sb[:, :, q0:q0 + HALF],
                                    gram_ps[:, b, 0:HALF * F].rearrange("p (q g) -> p g q", g=F)
                                    ).then_inc(gram_copied, 1)

            def copy_x(i, first):
                dve.wait_ge(turned_copied, (i + 1) * (PAIR * GROUPS))
                if not first:
                    dve.wait_ge(x_split, i * 2)
                dve.tensor_copy(x_sb.rearrange("d (j a q) -> d j a q", j=NJ, a=PAIR), xt_dense
                                ).then_inc(x_copied, 1)

            def split(i, first):
                for c in range(ZC):
                    dve.wait_ge(z_in[c], (i + 1) * (DMA * chunk_runs[c]))
                dve.wait_ge(x_copied, i + 1)
                if not first:
                    dve.wait_ge(mlp_ready, (i - 1) * U + C1)
                dve.tensor_copy(z_hi[:, :, :], z_sb[:, :, :]).then_inc(z_split, 1)
                dve.tensor_copy(x_hi[:, :], x_sb).then_inc(x_split, 1)
                dve.wait_ge(z_split, 2 * i + 1)
                dve.tensor_tensor(z_lo[:, :, :], z_sb[:, :, :], z_hi[:, :, :].bitcast(F32), ALU.subtract
                                  ).then_inc(z_split, 1)
                dve.wait_ge(x_split, 2 * i + 1)
                dve.tensor_tensor(x_lo[:, :], x_sb, x_hi[:, :].bitcast(F32), ALU.subtract
                                  ).then_inc(x_split, 1)

            def split_x_last(i):
                dve.wait_ge(x_copied, i + 1)
                dve.wait_ge(onehot_used, TURNS * (2 * NS))
                dve.tensor_copy(last_x_hi, x_sb).then_inc(x_split, 1)
                dve.wait_ge(x_split, 2 * i + 1)
                dve.tensor_tensor(last_x_lo, x_sb, last_x_hi.bitcast(F32), ALU.subtract).then_inc(x_split, 1)

            def split_z_last(i, c):
                if c == 0:
                    dve.wait_ge(mlp_ready, (i - 1) * U + C1)
                dve.wait_ge(z_in[c], (i + 1) * (DMA * chunk_runs[c]))
                dve.tensor_copy(z_hi[:, c, :], z_sb[:, c, :]).then_inc(z_split, 1)
                dve.wait_ge(z_split, 2 * (i + c) + 1)
                dve.tensor_tensor(z_lo[:, c, :], z_sb[:, c, :], z_hi[:, c, :].bitcast(F32), ALU.subtract
                                  ).then_inc(z_split, 1)

            def split_h1(i, u):
                dve.wait_ge(h1_hi_ready, i * C1 + u + 1)
                dve.tensor_tensor(h1_lo[:, u, :], h1[:, u % 2, :], h1_hi[:, u, :].bitcast(F32), ALU.subtract
                                  ).then_inc(h1_lo_ready, 1)

            def split_weights(m):
                k = NS + m
                if k < NST:
                    split_lo(k)
                elif k == NST:
                    dve.wait_ge(stage_in[NST % 2], (NST // 2 + 2) * DMA)
                    dve.tensor_tensor(w1s, w1s, stage[:, NST % 2, N1:2 * N1], ALU.add).then_inc(w1s_ready, 1)
                elif k == NST + 1:
                    dve.wait_ge(hi_ready, NST + 1)
                    dve.tensor_tensor(w1x_lo[:, :, :], by_unit(w1s, C1), w1x_hi[:, :, :].bitcast(F32), ALU.subtract
                                      ).then_inc(lo_ready, 1)

            def pair(i, first, last):
                for n in range(PARTS, 2 * NS):
                    make_onehot(i, n, False)
                    k = (n - 1 - PARTS) // 2
                    if n % 2 and k in LAYER1_AFTER and not first:
                        split_h1(i - 2, LAYER1_AFTER[k])
                    if n % 2 and first and (n - PARTS) // 2 < NST - NS:
                        split_weights((n - PARTS) // 2)
                if first:
                    split_weights(NST - NS)
                split(i - 1, first)
                if first:
                    split_weights(NST + 1 - NS)
                before = 0 if first else PARTS - 2
                if not last:
                    for n in range(before):
                        make_onehot(i + 1, n, False)
                copy_grams(i, 0, False)
                if not last:
                    for n in range(before, PARTS):
                        make_onehot(i + 1, n, False)
                copy_grams(i, 1, False)
                copy_x(i, False)

            for b in range(2):
                dve.memset(gram_ps[:, b, 0:HALF * F], 0.0).then_inc(gram_cleared, 1)
            dve.wait_ge(row_ids_ready, 1)
            dve.tensor_copy(row_ids_f[:, :], row_ids[:, :]).then_inc(row_ids_f_ready, 1)
            dve.wait_ge(row_ids_f_ready, 1)
            for k in range(NS):
                split_lo(k)
                for h in range(2):
                    make_onehot(0, 2 * k + h, True)
            for n in range(PARTS - 2):
                make_onehot(1, n, False)
            copy_grams(0, 0, True)
            for n in range(PARTS - 2, PARTS):
                make_onehot(1, n, False)
            copy_grams(0, 1, True)
            copy_x(0, True)
            pair(1, True, False)
            with dve.Fori(2, TURNS - 1) as i:
                pair(i, False, False)
            pair(TURNS - 1, False, True)
            split_x_last(TURNS - 1)
            for u in range(C1):
                split_h1(TURNS - 2, u)
            for c in range(ZC):
                split_z_last(TURNS - 1, c)
            for u in range(C1):
                split_h1(TURNS - 1, u)

        @block.tensor
        def _(pe):
            def select(i, k, first):
                if first:
                    pe.wait_ge(lo_ready, k + 1)
                if not (first and k < 2):
                    pe.wait_ge(selected_copied, i * NS + max(k - 1, 0))
                for h in range(2):
                    n = 2 * k + h
                    pe.wait_ge(onehot_ready, i * (2 * NS) + n + 1)
                    for c in range(VH):
                        for tab in (tab_hi, tab_lo):
                            c0 = (h * VH + c) * D
                            mm = pe.matmul(select_ps[:, k % 2, 0:COLS], tab[:, k, c0:c0 + D],
                                           onehot[:, n % PARTS, c, :],
                                           start=(c0 == 0 and tab is tab_hi),
                                           stop=(c0 == (VC - 1) * D and tab is tab_lo))
                    mm.then_inc(onehot_used, 1)

            def turn(i, t, first):
                a, g = t // GROUPS, t % GROUPS
                if g == 0:
                    pe.wait_ge(dense_in[a], (i + 1) * DMA)
                n = min(GROUP, R - g * GROUP)
                pe.wait_ge(gathered[a][g], (i + 1) * (DMA * (n - 1 if g == 0 else n)))
                if not (first and t < 2):
                    pe.wait_ge(turned_copied, i * (PAIR * GROUPS) + t - 1)
                for m in range(n):
                    mm = pe.transpose(turn_ps[:, t % 2, m * P:(m + 1) * P],
                                      rows_sb[:, a, g * GROUP + m, :], ident[:, :])
                mm.then_inc(turned, 1)

            def grams(i, a, first):
                pe.wait_ge(turned_copied, i * (PAIR * GROUPS) + (a + 1) * GROUPS)
                pe.wait_ge(selected_copied, (i + 1) * NS)
                for b in range(2):
                    if not (first and a == 0):
                        pe.wait_ge(gram_copied, i * (2 * PAIR) + 2 * a + b - 1)
                    for q in range(HALF):
                        for j in range(NJ):
                            p = j * QUAD + b * HALF + q
                            mm = pe.matmul(gram_ps[j * QUAD:j * QUAD + F, b, q * F:(q + 1) * F],
                                           xt[:, a, p, :], xt[:, a, p, :], start=True, stop=True,
                                           tile_position=(0, j * QUAD))
                    mm.then_inc(gram_ready, 1)

            def layer1(i, u, first):
                if u == 0:
                    pe.wait_ge(z_split, (i + 1) * 2)
                    pe.wait_ge(x_split, (i + 1) * 2)
                if not (first and u < 2):
                    pe.wait_ge(mlp_copied, i * U + max(u - 1, 0))
                o = mlp_ps[:, u % 2, 0:COLS]
                for c in range(ZC):
                    for n, (w, z) in enumerate(((w1z_hi, z_hi), (w1z_hi, z_lo), (w1z_lo, z_hi))):
                        pe.matmul(o, w[:, c, u, :], z[:, c, :], start=(c == 0 and n == 0), stop=False)
                for n, (w, x) in enumerate(((w1x_hi, x_hi), (w1x_hi, x_lo), (w1x_lo, x_hi))):
                    mm = pe.matmul(o, w[:, u, :], x[:, :], start=False, stop=(n == 2))
                mm.then_inc(mlp_ready, 1)

            def layer2(i, m):
                if m == 0:
                    pe.wait_ge(h1_lo_ready, (i + 1) * C1)
                u = C1 + m
                pe.wait_ge(mlp_copied, i * U + u - 1)
                for c in range(C1):
                    for n, (w, h) in enumerate(((w2_hi, h1_hi), (w2_hi, h1_lo), (w2_lo, h1_hi))):
                        mm = pe.matmul(mlp_ps[:, u % 2, 0:COLS], w[:, c, m, :], h[:, c, :],
                                       start=(c == 0 and n == 0), stop=(c == C1 - 1 and n == 2))
                mm.then_inc(mlp_ready, 1)

            def result(i):
                pe.wait_ge(mlp_copied, i * U + U - 1)
                for c in range(C2):
                    mm = pe.matmul(mlp_ps[0:1, (U - 1) % 2, 0:COLS], w3_sb[:, c:c + 1], h2[:, c, :],
                                   start=(c == 0), stop=(c == C2 - 1))
                mm.then_inc(mlp_ready, 1)

            def pair(i, first, mlp, first_mlp):
                done = 0
                for k in range(NS):
                    select(i, k, first)
                    for t in range(done, TURNED_BY[k]):
                        turn(i, t, first)
                    done = TURNED_BY[k]
                    if mlp and k in LAYER1_AFTER:
                        layer1(i - 2, LAYER1_AFTER[k], first_mlp)
                    if mlp and k in LAYER2_AFTER:
                        layer2(i - 2, LAYER2_AFTER[k])
                grams(i, 0, first)
                for t in range(done, PAIR * GROUPS):
                    turn(i, t, first)
                if mlp:
                    result(i - 2)
                grams(i, 1, first)

            def last_dense(i):
                pe.wait_ge(x_split, (i + 1) * 2)
                pe.wait_ge(selected_copied, TURNS * NS)
                pe.wait_ge(turned_copied, TURNS * (PAIR * GROUPS))
                for u in range(C1):
                    for n, (w, x) in enumerate(((w1x_hi, last_x_hi), (w1x_hi, last_x_lo), (w1x_lo, last_x_hi))):
                        pe.matmul(last_banks[u][:, 0:COLS], w[:, u, :], x, start=(n == 0), stop=False)

            def last_chunk(i, c):
                pe.wait_ge(z_split, 2 * (i + c) + 2)
                for u in range(C1):
                    for n, (w, z) in enumerate(((w1z_hi, z_hi), (w1z_hi, z_lo), (w1z_lo, z_hi))):
                        mm = pe.matmul(last_banks[u][:, 0:COLS], w[:, c, u, :], z[:, c, :], start=False,
                                       stop=(c == ZC - 1 and n == 2))
                    if c == ZC - 1:
                        mm.then_inc(last_ready, 1)

            def last_layer2(i):
                pe.wait_ge(gram_copied, TURNS * (2 * PAIR))
                for c in range(C1):
                    pe.wait_ge(h1_lo_ready, i * C1 + c + 1)
                    for m in range(C2):
                        for n, (w, h) in enumerate(((w2_hi, h1_hi), (w2_hi, h1_lo), (w2_lo, h1_hi))):
                            mm = pe.matmul(gram_ps[:, m, 0:COLS], w[:, c, m, :], h[:, c, :],
                                           start=(c == 0 and n == 0), stop=(c == C1 - 1 and n == 2))
                        if c == C1 - 1:
                            mm.then_inc(last_ready, 1)

            def last_result():
                for c in range(C2):
                    pe.wait_ge(last_copied, C1 + c + 1)
                    mm = pe.matmul(mlp_ps[0:1, 1, 0:COLS], w3_sb[:, c:c + 1], h2[:, c, :],
                                   start=(c == 0), stop=(c == C2 - 1))
                mm.then_inc(last_ready, 1)

            pe.wait_ge(ident_ready, 1)
            pe.wait_ge(gram_cleared, 2)
            pair(0, True, False, False)
            pair(1, False, False, False)
            pe.wait_ge(lo_ready, NST + 1)
            pe.wait_ge(small_in, 3 * DMA)
            pair(2, False, True, True)
            pair(3, False, True, False)
            with pe.Fori(4, TURNS, 2) as i:
                for k in range(2):
                    pair(i + k, False, True, False)
            for u in range(C1):
                layer1(TURNS - 2, u, False)
            last_dense(TURNS - 1)
            for m in range(C2):
                layer2(TURNS - 2, m)
            for c in range(ZC - 1):
                last_chunk(TURNS - 1, c)
            result(TURNS - 2)
            last_chunk(TURNS - 1, ZC - 1)
            last_layer2(TURNS - 1)
            last_result()


def kernel(**inputs):
    import numpy as np
    import concourse.bacc as bacc
    from concourse.bass_utils import run_bass_kernel_spmd as run

    B, NT = inputs["ids"].shape
    D = inputs["r_dense_features"].shape[1]
    rows, chosen = feature_order([inputs[f"tbl_{t}"].shape[0] for t in range(NT)])
    feature = [0] + [t + 1 for t in rows + chosen]
    F = NT + 1
    where = {}
    for a in range(F):
        for b in range(a + 1, F):
            where[a, b] = D + len(where)
    _, pairs = pair_order(F)
    order = [where[min(feature[a], feature[b]), max(feature[a], feature[b])] for a, b in pairs]
    w1 = inputs["W_top1"]
    order = list(range(D)) + order + list(range(D + len(order), w1.shape[0]))

    ids = np.asarray(inputs["ids"])
    given = {"dense": inputs["r_dense_features"], "ids_rows": ids[:, rows], "ids_cols": ids[:, chosen].T,
             "w1": np.asarray(w1)[order], "b1": inputs["b_top1"], "w2": inputs["W_top2"],
             "b2": inputs["b_top2"], "w3": inputs["W_top3"]}
    given.update({f"tbl_{t}": inputs[f"tbl_{t}"] for t in range(NT)})
    nc = bacc.Bacc("TRN2", target_bir_lowering=False, num_devices=1, dynamic_dma_scratch_size=8192)
    arrays, aps = {}, {}
    for name, a in given.items():
        a = np.ascontiguousarray(a)
        arrays["in_" + name] = a
        aps[name] = nc.dram_tensor("in_" + name, a.shape, mybir.dt.from_np(a.dtype), kind="ExternalInput").ap()
    out = nc.dram_tensor("out", (B, 1), F32, kind="ExternalOutput").ap()
    build_dlrm(nc, aps["dense"], aps["ids_rows"], aps["ids_cols"], [aps[f"tbl_{t}"] for t in rows],
               [aps[f"tbl_{t}"] for t in chosen], aps["w1"], aps["b1"], aps["w2"], aps["b2"], aps["w3"], out)
    r = run(nc, [arrays], core_ids=[0])
    return r.results[0]["out"]
```
